# Optimizing a Trainium2 kernel written in Bass

```python
import numpy as np
import jax
import jax.numpy as jnp

def _softmax(x, axis=-1):
    return jax.nn.softmax(x, axis=axis)
def _gelu(x):
    return jax.nn.gelu(x, approximate=True)
def _silu(x):
    return jax.nn.silu(x)
def _sigmoid(x):
    return jax.nn.sigmoid(x)
def _layernorm(x, axis=-1, eps=1e-5):
    m = jnp.mean(x, axis=axis, keepdims=True)
    v = jnp.var(x, axis=axis, keepdims=True)
    return (x - m) / jnp.sqrt(v + eps)
def _scatter_add(tgt, idx, src, axis=0):
    return tgt.at[idx].add(src)
def _segment_sum(src, seg, n):
    return jax.ops.segment_sum(src, seg, n)

kernel_name = 'mk_adj_resnorm_d1_adj_128_269211'

def setup_inputs(seed: int = 0):
    np.random.seed(seed)
    _w = jnp.asarray
    def _rec_inputs():
        import jax
        import jax.numpy as jnp
        _gk = jax.random.key(seed)
        x = -9.806e-05 + 1 * jax.random.normal(jax.random.fold_in(_gk, 1), (8192, 128), jnp.float32)
        _a = jax.random.bernoulli(jax.random.fold_in(_gk, 2), 0.00390625, (8192, 8192))
        _a = jnp.logical_or(_a, jnp.eye(8192, dtype=bool))
        _af = _a.astype(jnp.float32)
        _af = _af * jax.random.uniform(jax.random.fold_in(_gk, 3), (8192, 8192), jnp.float32, 0.05, 1)
        adj = _af
        return x, adj
    x, adj = _rec_inputs()
    def _L0_gnn_setup():
        import jax, jax.numpy as jnp
        import numpy as np

        def _lap_mul(A, x):
            d = 1.0 / jnp.sqrt(jnp.sum(A, axis=-1))
            return d[:, None] * (A @ (d[:, None] * x))
        key = jax.random.key(seed)
        k1, k2, k3, k4, k5, k6 = jax.random.split(key, 6)
        N, D_IN, D_OUT = (4096, 128, 128)
        x = jax.random.normal(k1, (N, D_IN), dtype=jnp.float32)
        A = jax.random.uniform(k2, (N, N), dtype=jnp.float32)
        s1 = 1.0 / np.sqrt(D_IN)
        W1 = jax.random.uniform(k3, (D_IN, D_OUT), minval=-s1, maxval=s1, dtype=jnp.float32)
        b1 = jax.random.uniform(k4, (D_OUT,), minval=-s1, maxval=s1, dtype=jnp.float32)
        W2 = jax.random.uniform(k5, (D_IN, D_OUT), minval=-s1, maxval=s1, dtype=jnp.float32)
        b2 = jax.random.uniform(k6, (D_OUT,), minval=-s1, maxval=s1, dtype=jnp.float32)
        return {'x': x, 'A': A, 'W1': W1, 'b1': b1, 'W2': W2, 'b2': b2, 'sigma': 1, 'k': 4}
    _L0_gnn_all = _L0_gnn_setup()
    _L0_gnn_in = {k: v for k, v in _L0_gnn_all.items() if k in ('W1', 'b1', 'W2', 'b2', )}
    del _L0_gnn_all

    return {
        "x": x,
        "adj": adj,
        "L0_gnn_W1": _L0_gnn_in["W1"],
        "L0_gnn_b1": _L0_gnn_in["b1"],
        "L0_gnn_W2": _L0_gnn_in["W2"],
        "L0_gnn_b2": _L0_gnn_in["b2"],
    }

def reference(x, adj, L0_gnn_W1, L0_gnn_b1, L0_gnn_W2, L0_gnn_b2):
    import jax
    import jax.numpy as jnp
    def _L0_gnn_ref(x, A, W1, b1, W2, b2, sigma, k):
        import jax, jax.numpy as jnp
        import numpy as np

        def _lap_mul(A, x):
            d = 1.0 / jnp.sqrt(jnp.sum(A, axis=-1))
            return d[:, None] * (A @ (d[:, None] * x))
        z = _lap_mul(A, x) @ W1 + b1
        z = jax.nn.leaky_relu(z, negative_slope=0.1)
        sq = jnp.sum(z * z, axis=-1)
        d2 = sq[:, None] + sq[None, :] - 2.0 * (z @ z.T)
        d2 = jnp.maximum(d2, 0.0)
        S = jnp.sqrt(d2 + 1e-10)
        S = jnp.exp(-S / (2.0 * sigma))
        order = jnp.argsort(-S, axis=-1)
        ranks = jnp.argsort(order, axis=-1)
        S = jnp.where(ranks < k, S, 0.0)
        A2 = S + A
        out = _lap_mul(A2, x) @ W2 + b2
        return out

    x = _layernorm(x + _L0_gnn_ref(x, adj, L0_gnn_W1, L0_gnn_b1, L0_gnn_W2, L0_gnn_b2, 1, 4), axis=-1)
    return x


_drawn_inputs = setup_inputs


def setup_inputs(seed=0):
    import zlib

    import numpy as np

    out = dict(_drawn_inputs(seed))
    spreads = {}
    factors = {}
    for name, (base, spread) in spreads.items():
        noise = np.random.default_rng([zlib.crc32(name.encode()), seed]).standard_normal(out[name].shape)
        drawn = base * np.exp(spread * noise) if base else spread * noise
        out[name] = jnp.asarray(drawn.astype(out[name].dtype))
    for name, factor in factors.items():
        out[name] = (out[name] * factor).astype(out[name].dtype)
    return out
```

```python
import numpy as np
import concourse.bass as bass
from concourse import mybir
from contextlib import ExitStack

F32 = mybir.dt.float32
F32R = mybir.dt.float32r
U32 = mybir.dt.uint32
ALU = mybir.AluOpType
ACT = mybir.ActivationFunctionType
AX = mybir.AxisListType.X

N, D, P = 8192, 128, 128
T = N // P
BC = 512
B = N // BC
TB = BC // P
KNN, TOP = 4, 8
GT = 8
G = T // GT
HB = B // 2
EC = 2 * BC
NE = N // EC
SQH = B // 2
SLOTS_A, SLOTS_B = 7, 4
SLOT = TB * BC
LN_EPS, D2_EPS, SLOPE = 1e-5, 1e-10, 0.1

C_ID, C_WIN = 0, P
WIN = P + 2 * (SQH - 1)
C_E = C_WIN + WIN
C_MASK = C_E + SQH * P
C_ALL = C_MASK + 2


def constants():
    c = np.zeros((P, C_ALL), np.float32)
    c[:, C_ID:C_ID + P] = np.eye(P)
    c[:, C_WIN + 2 * (SQH - 1):C_WIN + 2 * SQH] = -0.5
    for k in range(SQH):
        c[2 * k:2 * k + 2, C_E + k * P:C_E + (k + 1) * P] = 1.0
    c[0::2, C_MASK] = 1.0
    c[1::2, C_MASK + 1] = 1.0
    return c


def plan_ab():
    one = [(b, (b + 1 + i) % B) for b in range(B) for i in range(B)]
    two = [(b, q) for b in reversed(range(B)) for q in range(b + 1, B)]
    return one, two


def build(nc, x, at, W1, b1, W2, b2, consts, out, xs_dram):
    one, two = plan_ab()
    n_one = len(one)
    ctx = ExitStack()
    with ctx:
        def sb(name, shape, dt=F32):
            return ctx.enter_context(nc.sbuf_tensor(name, shape, dt))

        def sem(name):
            return ctx.enter_context(nc.semaphore(name))

        R1 = sb("R1", [P, 2 * N])
        R2 = sb("R2", [P, N])
        ring = sb("ring", [P, SLOTS_B, TB, BC])
        zh = sb("zh", [P, N], F32R)
        zl = sb("zl", [P, N], F32R)
        sqn = sb("sqn", [P, 2, BC], F32R)
        sel = sb("sel", [P, SQH, P], F32R)
        zst = sb("zst", [P, 2, 2, P], F32R)
        ident = sb("ident", [P, P])
        w1 = sb("w1", [P, D])
        w2 = sb("w2", [P, D])
        b1r = sb("b1r", [P, D])
        b2r = sb("b2r", [P, D])
        masks = sb("masks", [P, 2])
        ones = sb("ones", [P, 1])
        rowsum = sb("rowsum", [P, T])
        dsc = sb("dsc", [P, T])
        sq = sb("sq", [P, T])
        d2s = sb("d2s", [P, T])
        tiny = sb("tiny", [P, 5, GT])

        xs = R1[:, 0:N].rearrange("p (t d) -> p t d", d=D)
        slots_a = [ring[:, s] for s in range(SLOTS_B)]
        for s in range(SLOTS_A - SLOTS_B):
            slots_a.append(R1[:, N + s * SLOT:N + (s + 1) * SLOT].rearrange("p (k c) -> p k c", k=TB))
        tmp = R1[:, N + (SLOTS_A - SLOTS_B) * SLOT:2 * N]
        part = [tmp[:, 0:BC], tmp[:, BC:2 * BC]]
        e_raw = tmp[:, 0:SQH * P]
        y = tmp[:, 0:BC]
        zn = tmp[:, BC:2 * BC].rearrange("p (j d) -> p j d", j=TB)
        window = tmp[:, 2 * BC:2 * BC + WIN]
        junk = tmp[:, 2 * BC + 256:2 * BC + 256 + P]
        z2 = tmp[:, 3 * BC:4 * BC]
        score = [R1[:, 0:N], R1[:, N:2 * N]]
        acc = R2[:, 0:HB * BC]
        at_ = [HB * BC]

        def cut(n):
            at_[0] += n
            return R2[:, at_[0] - n:at_[0]]

        xg = cut(GT * D).rearrange("p (j d) -> p j d", j=GT)
        xn = cut(GT * D).rearrange("p (j d) -> p j d", j=GT)
        flush = [cut(BC), cut(BC)]
        top = cut(GT * TOP).rearrange("p (j m) -> p j m", j=GT)
        place = cut(GT * TOP).bitcast(U32).rearrange("p (j m) -> p j m", j=GT)
        dist = cut(GT * KNN).rearrange("p (j m) -> p j m", j=GT)
        near = cut(GT * KNN).rearrange("p (j m) -> p j m", j=GT)
        sval = cut(T * KNN).rearrange("p (t m) -> p t m", t=T)
        sidx = cut(T * KNN).bitcast(U32).rearrange("p (t m) -> p t m", t=T)
        xsc = R1[:, 0:N].rearrange("p (t d) -> p t d", d=D)
        bt = [N]

        def cut1(n):
            bt[0] += n
            return R1[:, bt[0] - n:bt[0]]

        gx = [cut1(TB * KNN * D).rearrange("p (j m d) -> p (j m) d", j=TB, m=KNN) for _ in range(2)]
        gs = [cut1(BC).rearrange("p (j d) -> p j d", j=TB) for _ in range(2)]
        yf = [cut1(BC) for _ in range(2)]
        xb = [cut1(BC).rearrange("p (j d) -> p j d", j=TB) for _ in range(2)]
        res = [cut1(BC).rearrange("p (j d) -> p j d", j=TB) for _ in range(2)]
        small = sb("small", [P, TB * (2 * 2 * KNN + 2 + 6 + 2 + 1)])
        ct = [0]

        def cut2(n):
            ct[0] += n
            return small[:, ct[0] - n:ct[0]]

        gidx = [cut2(TB * KNN).bitcast(U32) for _ in range(2)]
        gval = [cut2(TB * KNN) for _ in range(2)]
        gd2 = [cut2(TB) for _ in range(2)]
        stats = cut2(TB * 6).rearrange("p (j s) -> p j s", j=TB)
        mv = cut2(TB * 2).rearrange("p (j s) -> p j s", j=TB)
        rstd = cut2(TB)

        PS = ctx.enter_context(nc.psum_tensor("PS", [P, 8, BC], F32))

        gate = sem("gate")
        s_const = sem("s_const")
        s_x = sem("s_x")
        ld_a = [sem(f"ld_a{s}") for s in range(SLOTS_A)]
        const_ok = sem("const_ok")
        reduced = sem("reduced")
        summed = sem("summed")
        diag_done = sem("diag_done")
        sums_read = sem("sums_read")
        root_ok = sem("root_ok")
        xs_ok = sem("xs_ok")
        y_saved = sem("y_saved")
        prod2 = sem("prod2")
        y_ok = sem("y_ok")
        zraw = sem("zraw")
        zn_ok = sem("zn_ok")
        sq_ok = sem("sq_ok")
        zt = sem("zt")
        z2_ok = sem("z2_ok")
        zl_ok = sem("zl_ok")
        sqs = sem("sqs")
        sqn_ok = sem("sqn_ok")
        dve = sem("dve")
        dve3 = sem("dve3")
        dve4 = sem("dve4")
        act1 = sem("act1")
        st_ok = sem("st_ok")
        gram = sem("gram")
        copied = sem("copied")
        placed = sem("placed")
        dist_ok = sem("dist_ok")
        near_ok = sem("near_ok")
        act3 = sem("act3")
        r2_ok = sem("r2_ok")
        root2_ok = sem("root2_ok")
        s_xn = sem("s_xn")
        xg_ok = sem("xg_ok")
        s_xg = sem("s_xg")
        acc0 = sem("acc0")
        ld_b = [sem(f"ld_b{s}") for s in range(SLOTS_B)]
        prodb = sem("prodb")
        flushed = sem("flushed")
        added = sem("added")
        s_xsc = sem("s_xsc")
        gi_ok = sem("gi_ok")
        s_gx = [sem(f"s_gx{k}") for k in range(2)]
        gs_ok = sem("gs_ok")
        u_ok = sem("u_ok")
        yf_ok = sem("yf_ok")
        v_ok = sem("v_ok")
        s_xb = [sem(f"s_xb{k}") for k in range(2)]
        res_free = sem("res_free")
        var_ok = sem("var_ok")
        std_ok = sem("std_ok")
        out_ok = sem("out_ok")
        s_out = [sem(f"s_out{k}") for k in range(2)]

        block = ctx.enter_context(nc.Block())

        class Link:
            def __init__(self, eng, own, base):
                self.eng, self.own, self.base, self.n = eng, own, base, 0

            def __call__(self, ins):
                self.n += 1
                ins.then_inc(self.own, 1)
                self.eng.wait_ge(self.own, self.base + self.n)

        def hold(eng):
            eng.sem_inc(gate, 1)

        def bcast(ap, n):
            return ap.unsqueeze(len(ap.shape)).to_broadcast(list(ap.shape) + [n])

        def newton(link, r, root, y0, a, y1):
            link(nc.vector.reciprocal(y0, root))
            link(nc.vector.tensor_tensor(a, y0, y0, ALU.mult))
            link(nc.vector.tensor_tensor(a, a, r, ALU.mult))
            link(nc.vector.tensor_scalar(a, a, -0.5, 1.5, ALU.mult, ALU.add))
            link(nc.vector.tensor_tensor(y1, y0, a, ALU.mult))

        blocks2 = list(reversed(range(B)))
        last_quad = {}
        for n, (b, q) in enumerate(two):
            last_quad[b] = n + 1
        CH3 = 10
        FIRST4 = G * HB * 2

        UNITS = [[], [0], [1], [2], [3], [4], [5], [6, 7]]

        @block.sync
        def _(sp):
            sp.dma_start(ident[:, :], consts[:, C_ID:C_ID + P]).then_inc(s_const, 16)
            sp.dma_start(e_raw, consts[:, C_E:C_E + SQH * P]).then_inc(s_const, 16)
            sp.dma_start(window, consts[:, C_WIN:C_WIN + WIN]).then_inc(s_const, 16)
            sp.dma_start(masks[:, :], consts[:, C_MASK:C_MASK + 2]).then_inc(s_const, 16)
            sp.dma_start(w1[:, :], W1).then_inc(s_const, 16)
            sp.dma_start(w2[:, :], W2).then_inc(s_const, 16)
            sp.dma_start(b1r[:, :], b1.partition_broadcast(P)).then_inc(s_const, 16)
            sp.dma_start(b2r[:, :], b2.partition_broadcast(P)).then_inc(s_const, 16)
            for n, (b, q) in enumerate(one + two):
                m = n - SLOTS_A
                if m >= n_one:
                    sp.wait_ge(prod2, m - n_one + 1)
                elif m >= 0:
                    sp.wait_ge(summed, m + 1)
                    if m % B == B - 1:
                        sp.wait_ge(diag_done, m // B + 1)
                sp.dma_start(slots_a[n % SLOTS_A], at[b, :, q * TB:(q + 1) * TB, :])\
                  .then_inc(ld_a[n % SLOTS_A], 16)
                if n == 1:
                    sp.dma_start(xs, x.rearrange("(t p) d -> p t d", p=P)).then_inc(s_x, 16)

            sp.wait_ge(prod2, len(two))
            sp.wait_ge(y_ok, B)
            sp.dma_start(xn, x[0:GT * P].rearrange("(t p) d -> p t d", p=P)).then_inc(s_xn, 16)

            def group_loads(g, first):
                for ib in range(HB):
                    for h in range(2):
                        k = 2 * ib + h
                        slot = k % SLOTS_B
                        if not first or k >= SLOTS_B:
                            sp.wait_ge(prodb, g * (2 * HB) + (k - SLOTS_B + 1))
                        src = at[ib, :, bass.ds(g * GT + h * TB, TB), :]
                        sp.dma_start(ring[:, slot], src).then_inc(ld_b[slot], 16)
                        if k == SLOTS_B - 1:
                            sp.wait_ge(xg_ok, g + 1)
                            dst = xs_dram[bass.ds(g * GT * P, GT * P)]
                            sp.dma_start(dst.rearrange("(t p) d -> p t d", p=P), xg).then_inc(s_xg, 16)
                            if not (isinstance(g, int) and g == G - 1):
                                src = x[bass.ds((g + 1) * GT * P, GT * P)]
                                sp.dma_start(xn, src.rearrange("(t p) d -> p t d", p=P)).then_inc(s_xn, 16)

            group_loads(0, True)
            with sp.Fori(1, G - 1) as g:
                group_loads(g, False)
            group_loads(G - 1, False)

            sp.wait_ge(s_xg, 16 * G)
            sp.wait_ge(placed, T)
            sp.dma_start(xsc, xs_dram.rearrange("(t p) d -> p t d", p=P)).then_inc(s_xsc, 16)

            def step_loads(s):
                for h in range(B):
                    slot = h % SLOTS_B
                    sp.wait_ge(prodb, FIRST4 + s * B + (h - SLOTS_B + 1))
                    src = at[bass.ds(HB + s, 1), :, h * TB:(h + 1) * TB, :]
                    sp.dma_start(ring[:, slot], src.rearrange("o p k c -> p (o k) c")).then_inc(ld_b[slot], 16)
                    if h == 6:
                        for k in range(2):
                            row = (HB + s if k == 0 else s) * BC
                            if isinstance(s, int) and s == 0:
                                pass
                            else:
                                sp.wait_ge(res_free, 2 * s - 1 + k)
                            sp.dma_start(xb[k], x[bass.ds(row, BC)].rearrange("(t p) d -> p t d", p=P))\
                              .then_inc(s_xb[k], 16)

            def step_stores(s):
                for k in range(2):
                    row = (HB + s if k == 0 else s) * BC
                    sp.wait_ge(out_ok, 2 * s + k + 1)
                    sp.dma_start(out[bass.ds(row, BC)].rearrange("(t p) d -> p t d", p=P), res[k])\
                      .then_inc(s_out[k], 16)

            step_loads(0)
            with sp.Fori(1, HB) as s:
                step_loads(s)
                step_stores(s - 1)
            step_stores(HB - 1)
            for k in range(2):
                sp.wait_ge(s_out[k], 16 * HB)

        @block.tensor
        def _(pe):
            pe.wait_ge(const_ok, 1)
            for n, (b, q) in enumerate(one):
                prod, sums = PS[:, b % 2], PS[:, 2 + b % 2]
                tile = slots_a[n % SLOTS_A]
                pe.wait_ge(ld_a[n % SLOTS_A], 16 * (n // SLOTS_A + 1))

                def products(first, last):
                    pe.wait_ge(xs_ok, q + 1)
                    if first and b >= 2:
                        pe.wait_ge(y_saved, b - 1)
                    for k in range(TB):
                        i = pe.matmul(prod, xs[:, q * TB + k], tile[:, k], start=first and k == 0,
                                      stop=last and k == TB - 1)
                    return i

                if q < b:
                    products(q == 0, False)
                pe.wait_ge(reduced, n + 1)
                if n % B == 0 and b >= 2:
                    pe.wait_ge(sums_read, b - 1)
                for j in range(TB):
                    i = pe.matmul(sums[:, j:j + 1], part[n % 2][:, j * P:(j + 1) * P], ones[:, :],
                                  start=n % B == 0 and j == 0, stop=n % B == B - 1 and j == TB - 1,
                                  skip_group_check=True)
                i.then_inc(summed, 1)
                if q == b:
                    products(b == 0, True).then_inc(diag_done, 1)

            def z_raw(pi):
                b = blocks2[pi]
                pe.wait_ge(y_ok, pi + 1)
                if pi >= 1:
                    pe.wait_ge(zn_ok, pi)
                for j in range(TB):
                    i = pe.matmul(PS[:, 4, j * P:(j + 1) * P], y[:, j * P:(j + 1) * P], w1[:, :],
                                  start=True, stop=True)
                i.then_inc(zraw, 1)

            def z_transposed(pi):
                pe.wait_ge(zn_ok, pi + 1)
                if pi >= 1:
                    pe.wait_ge(zl_ok, pi)
                    pe.wait_ge(z2_ok, pi)
                for j in range(TB):
                    i = pe.transpose(PS[:, 5, j * P:(j + 1) * P], zn[:, j], ident[:, :])
                i.then_inc(zt, 1)

            def squares(pi):
                b = blocks2[pi]
                k = b % SQH
                pe.wait_ge(z2_ok, pi + 1)
                pe.matmul(PS[:, 6 + b // SQH], window[:, 2 * (SQH - 1 - k):2 * (SQH - 1 - k) + P], z2,
                          start=k == SQH - 1, stop=k == 0).then_inc(sqs, 1)

            n = n_one
            for pi, b in enumerate(blocks2):
                prod = PS[:, pi % 2]
                if pi >= 1:
                    if pi >= 3:
                        pe.wait_ge(y_ok, pi - 1)
                    else:
                        pe.wait_ge(y_saved, B)
                for q in range(b + 1, B):
                    pe.wait_ge(ld_a[n % SLOTS_A], 16 * (n // SLOTS_A + 1))
                    for k in range(TB):
                        i = pe.matmul(prod, xs[:, q * TB + k], slots_a[n % SLOTS_A][:, k],
                                      start=q == b + 1 and k == 0, stop=q == B - 1 and k == TB - 1)
                    i.then_inc(prod2, 1)
                    n += 1
                if pi >= 1:
                    z_raw(pi - 1)
                if pi >= 2:
                    z_transposed(pi - 2)
                if pi >= 3:
                    squares(pi - 3)
            z_raw(B - 1)
            z_transposed(B - 2)
            squares(B - 3)
            z_transposed(B - 1)
            squares(B - 2)
            squares(B - 1)

            def scores(g, j, first):
                par = j % 2
                pe.wait_ge(st_ok, 2 * (GT * g + j) + 2)
                for c in range(NE):
                    if not (first and j == 0 and c < 2):
                        pe.wait_ge(copied, NE * (GT * g + j) + c - 1)
                    for h in range(2):
                        cc = 2 * c + h
                        bank = PS[:, 2 * (c % 2) + h]
                        cols = slice(cc * BC, (cc + 1) * BC)
                        pe.matmul(bank, zst[:, par, 0], zh[:, cols], start=True, stop=False)
                        pe.matmul(bank, zst[:, par, 0], zl[:, cols], start=False, stop=False)
                        pe.matmul(bank, zst[:, par, 1], zh[:, cols], start=False, stop=False)
                        i = pe.matmul(bank, sel[:, cc % SQH], sqn[:, cc // SQH], start=False, stop=True)
                    i.then_inc(gram, 1)

            def unit(g, ib, first):
                bank = PS[:, 4 + ib % 2]
                if not (first and ib < 2):
                    pe.wait_ge(flushed, HB * g + ib - 1)
                if ib == 0:
                    pe.wait_ge(xg_ok, g + 1)
                for h in range(2):
                    k = 2 * ib + h
                    slot = k % SLOTS_B
                    pe.wait_ge(ld_b[slot], 16 * ((2 * HB // SLOTS_B) * g + k // SLOTS_B + 1))
                    for kk in range(TB):
                        i = pe.matmul(bank, xg[:, h * TB + kk], ring[:, slot, kk],
                                      start=h == 0 and kk == 0, stop=h == 1 and kk == TB - 1)
                    i.then_inc(prodb, 1)

            def group_pe(g, first):
                for j in range(GT):
                    scores(g, j, first)
                    if not first:
                        for ib in UNITS[j]:
                            unit(g - 1, ib, isinstance(g, int) and g == 1)

            pe.wait_ge(sqn_ok, 1)
            group_pe(0, True)
            group_pe(1, False)
            with pe.Fori(2, G) as g:
                group_pe(g, False)
            for ib in range(HB):
                unit(G - 1, ib, False)

            pe.wait_ge(s_xsc, 16)
            pe.wait_ge(flushed, HB * G)

            def step_pe(s, first):
                for k in range(2):
                    u, g_rows = PS[:, k], gs[k]
                    if k == 0:
                        if not first:
                            pe.wait_ge(yf_ok, 2 * s - 1)
                        for h in range(B):
                            slot = h % SLOTS_B
                            pe.wait_ge(ld_b[slot], 16 * (2 * HB // SLOTS_B * G + (B // SLOTS_B) * s + h // SLOTS_B + 1))
                            for kk in range(TB):
                                i = pe.matmul(u, xsc[:, h * TB + kk], ring[:, slot, kk],
                                              start=h == 0 and kk == 0, stop=h == B - 1 and kk == TB - 1)
                            i.then_inc(prodb, 1)
                    elif not first:
                        pe.wait_ge(yf_ok, 2 * s)
                    pe.wait_ge(gs_ok, 2 * s + k + 1)
                    for j in range(TB):
                        i = pe.matmul(u[:, j * P:(j + 1) * P], g_rows[:, j], ident[:, :],
                                      start=k == 1, stop=True, skip_group_check=True)
                    i.then_inc(u_ok, 1)
                    pe.wait_ge(yf_ok, 2 * s + k + 1)
                    if not first:
                        pe.wait_ge(var_ok, 2 * s - 1 + k)
                    for j in range(TB):
                        i = pe.matmul(PS[:, 2 + k, j * P:(j + 1) * P], yf[k][:, j * P:(j + 1) * P], w2[:, :],
                                      start=True, stop=True)
                    i.then_inc(v_ok, 1)

            step_pe(0, True)
            with pe.Fori(1, HB) as s:
                step_pe(s, False)

        @block.scalar
        def _(act):
            for b in range(B):
                act.wait_ge(sums_read, b + 1)
                act.activation(tiny[:, 0, 0:TB], rowsum[:, b * TB:(b + 1) * TB], ACT.Sqrt).then_inc(root_ok, 1)
                act.wait_ge(diag_done, b + 1)
                act.activation(R2[:, b * BC:(b + 1) * BC], PS[:, b % 2], ACT.Copy).then_inc(y_saved, 1)
                if b < B - 1:
                    act.wait_ge(xs_ok, b + 1)

            def z_squares(pi):
                b = blocks2[pi]
                act.wait_ge(zn_ok, pi + 1)
                for j in range(TB):
                    if pi + j:
                        act.wait_ge(sq_ok, TB * pi + j)
                    act.activation(junk, zn[:, j], ACT.Square,
                                   accum_out=sq[:, b * TB + j:b * TB + j + 1]).then_inc(sq_ok, 1)

            def z_split(pi):
                b = blocks2[pi]
                act.wait_ge(zt, pi + 1)
                act.activation(zh[:, b * BC:(b + 1) * BC], PS[:, 5], ACT.Copy)
                if pi >= 1:
                    act.wait_ge(sqs, pi)
                act.activation(z2, PS[:, 5], ACT.Square).then_inc(z2_ok, 1)

            for pi in range(B):
                z_squares(pi)
                z_split(pi)

            def group_act(g, first, chain):
                for j in range(GT):
                    for c in range(NE):
                        if c == 0 and not (first and j < 2):
                            act.wait_ge(placed, GT * g + j - 1)
                        if c == 0 and first and j == 0:
                            act.wait_ge(prod2, len(two))
                            act.wait_ge(sqs, B)
                        act.wait_ge(gram, NE * (GT * g + j) + c + 1)
                        act.activation(score[j % 2][:, c * EC:(c + 1) * EC],
                                       PS[:, 2 * (c % 2):2 * (c % 2) + 2].rearrange("p b c -> p (b c)"),
                                       ACT.Copy).then_inc(copied, 1)
                        if chain and j == 1 and c == 1:
                            s_of_distances(g - 1)
                        if chain and j == 1 and c == 2:
                            root_of_sums(g - 1)
                    if chain:
                        for ib in UNITS[j]:
                            flush_unit(g - 1, ib, isinstance(g, int) and g == 1)

            def s_of_distances(g):
                act.wait_ge(dist_ok, g + 1)
                act.activation(dist, dist, ACT.Sqrt).then_inc(act3, 1)
                act.wait_ge(act3, g + 1)
                act.activation(near, dist, ACT.Exp, scale=-0.5).then_inc(near_ok, 1)

            def root_of_sums(g):
                act.wait_ge(r2_ok, g + 1)
                act.activation(tiny[:, 1], tiny[:, 0], ACT.Sqrt).then_inc(root2_ok, 1)

            def flush_unit(g, ib, first):
                act.wait_ge(prodb, 2 * (HB * g + ib) + 2)
                if not (first and ib < 2):
                    act.wait_ge(added, HB * g + ib - 1)
                act.activation(flush[ib % 2], PS[:, 4 + ib % 2], ACT.Copy).then_inc(flushed, 1)

            group_act(0, True, False)
            group_act(1, False, True)
            with act.Fori(2, G) as g:
                group_act(g, False, True)
            s_of_distances(G - 1)
            root_of_sums(G - 1)
            for ib in range(HB):
                flush_unit(G - 1, ib, False)

            def step_act(s, first):
                for k in range(2):
                    act.wait_ge(u_ok, 2 * s + k + 1)
                    if not first:
                        act.wait_ge(v_ok, 2 * s - 1 + k)
                    if k == 0:
                        act.activation(yf[0], PS[:, 0], ACT.Copy).then_inc(yf_ok, 1)
                    act.wait_ge(var_ok, 2 * s + k + 1)
                    act.activation(rstd, mv[:, :, 1], ACT.Sqrt).then_inc(std_ok, 1)

            step_act(0, True)
            with act.Fori(1, HB) as s:
                step_act(s, False)

        @block.gpsimd
        def _(pool):
            def stationary(g, j, first):
                if not (first and j < 2):
                    pool.wait_ge(gram, NE * (GT * g + j - 1))
                    hold(pool)
                t = (GT * g + j) * P
                pool.tensor_copy(zst[:, j % 2, 0], zh[:, bass.ds(t, P)]).then_inc(st_ok, 1)
                pool.tensor_copy(zst[:, j % 2, 1], zl[:, bass.ds(t, P)]).then_inc(st_ok, 1)

            def add_unit(g, ib):
                pool.wait_ge(flushed, HB * g + ib + 1)
                cols = acc[:, ib * BC:(ib + 1) * BC]
                if not isinstance(g, int) or g or ib:
                    pool.wait_ge(added, HB * g + ib)
                pool.tensor_tensor(cols, cols, flush[ib % 2], ALU.add).then_inc(added, 1)

            def group_pool(g, first, units):
                for j in range(GT):
                    if j < GT - 1:
                        stationary(g, j + 1, first)
                    elif not (isinstance(g, int) and g == G - 1):
                        stationary(g + 1, 0, False)
                    if units:
                        for ib in UNITS[j]:
                            add_unit(g - 1, ib)

            pool.wait_ge(z2_ok, B)
            pool.wait_ge(zl_ok, B)
            pool.wait_ge(y_ok, B)
            stationary(0, 0, True)
            pool.wait_ge(acc0, 1)
            group_pool(0, True, False)
            group_pool(1, False, True)
            with pool.Fori(2, G - 1) as g:
                group_pool(g, False, True)
            group_pool(G - 1, False, True)
            for ib in range(HB):
                add_unit(G - 1, ib)

            pool.wait_ge(s_xg, 16 * G)

            def step_pool(s, first):
                for k in range(2):
                    pool.wait_ge(gi_ok, 2 * s + k + 1)
                    hold(pool)
                    for i in range(TB * KNN):
                        pool.indirect_dma_start(
                            gx[k][:, i], None, xs_dram,
                            bass.IndirectOffsetOnAxis(ap=gidx[k][:, i:i + 1], axis=0)).then_inc(s_gx[k], 16)

            step_pool(0, True)
            with pool.Fori(1, HB) as s:
                step_pool(s, False)

        @block.vector
        def _(v):
            link = Link(v, dve, 0)
            v.memset(ones[:, :], 1.0).then_inc(dve, 1)
            link.n += 1
            v.wait_ge(s_const, 16 * 8)
            link(v.tensor_copy(sel[:, :, :].rearrange("p k m -> p (k m)"), e_raw))
            v.sem_inc(const_ok, 1)
            v.wait_ge(s_x, 16)

            for n, (b, q) in enumerate(one):
                if n >= 2:
                    v.wait_ge(summed, n - 1)
                v.wait_ge(ld_a[n % SLOTS_A], 16 * (n // SLOTS_A + 1))
                v.tensor_reduce(part[n % 2], slots_a[n % SLOTS_A].rearrange("p k c -> p c k"), AX, ALU.add)\
                 .then_inc(reduced, 1)
                if q != b:
                    continue
                v.wait_ge(summed, n + 1)
                cols = slice(b * TB, (b + 1) * TB)
                v.tensor_copy(rowsum[:, cols], PS[:, 2 + b % 2, 0:TB]).then_inc(sums_read, 1)
                v.wait_ge(sums_read, b + 1)
                v.wait_ge(root_ok, b + 1)
                newton(link, rowsum[:, cols], tiny[:, 0, 0:TB], tiny[:, 1, 0:TB], tiny[:, 2, 0:TB], dsc[:, cols])
                v.tensor_tensor(xs[:, cols], xs[:, cols], bcast(dsc[:, cols], D), ALU.mult).then_inc(xs_ok, 1)

            def make_y(pi):
                b = blocks2[pi]
                v.wait_ge(y_saved, B if b == B - 1 else B)
                if pi == 0:
                    v.wait_ge(summed, n_one)
                else:
                    v.wait_ge(zraw, pi)
                cols = R2[:, b * BC:(b + 1) * BC]
                if b == B - 1:
                    v.tensor_copy(y, cols).then_inc(y_ok, 1)
                else:
                    v.wait_ge(prod2, last_quad[b])
                    v.tensor_tensor(y, cols, PS[:, pi % 2], ALU.add).then_inc(y_ok, 1)

            def make_z(pi):
                b = blocks2[pi]
                v.wait_ge(zraw, pi + 1)
                if pi >= 1:
                    v.wait_ge(zt, pi)
                    v.wait_ge(sq_ok, TB * pi)
                for j in range(TB):
                    t = b * TB + j
                    i = v.scalar_tensor_tensor(zn[:, j], PS[:, 4, j * P:(j + 1) * P], dsc[:, t:t + 1], b1r[:, :],
                                               ALU.mult, ALU.add)
                link(i)
                v.scalar_tensor_tensor(zn, zn, SLOPE, zn, ALU.mult, ALU.max).then_inc(zn_ok, 1)

            def make_zl(pi):
                b = blocks2[pi]
                cols = slice(b * BC, (b + 1) * BC)
                v.wait_ge(z2_ok, pi + 1)
                v.tensor_tensor(zl[:, cols], PS[:, 5], zh[:, cols].bitcast(F32), ALU.subtract).then_inc(zl_ok, 1)

            for pi in range(B):
                make_y(pi)
                if pi >= 1:
                    make_zl(pi - 1)
                make_z(pi)
            make_zl(B - 1)
            v.wait_ge(y_ok, B)
            v.memset(acc, 0.0).then_inc(acc0, 1)
            v.wait_ge(sqs, B)
            for h in range(2):
                hi = tmp[:, h * BC:(h + 1) * BC]
                link(v.tensor_copy(sqn[:, h], PS[:, 6 + h]))
                link(v.tensor_tensor(hi, PS[:, 6 + h], sqn[:, h].bitcast(F32), ALU.subtract))
                link(v.tensor_scalar(hi, hi, masks[:, 1:2], None, ALU.mult))
                link(v.scalar_tensor_tensor(sqn[:, h], sqn[:, h].bitcast(F32), masks[:, 0:1], hi, ALU.mult, ALU.add))
            v.sem_inc(sqn_ok, 1)

            def find(g, j):
                lk = Link(v, placed, GT * g + j)
                v.wait_ge(copied, NE * (GT * g + j + 1))
                hold(v)
                v.max(top[:, j], score[j % 2]).then_inc(dve3, 1)
                v.wait_ge(dve3, (GT + CH3) * g + j + 1)
                hold(v)
                lk(v.max_index(place[:, j], top[:, j], score[j % 2]))

            def chain(g):
                lk = Link(v, dve3, (GT + CH3) * g + GT)
                tiles, d2g = bass.ds(g * GT, GT), tiny[:, 4]
                lk(v.tensor_scalar(dist, top[:, :, 0:KNN], -2.0, None, ALU.mult))
                lk(v.tensor_tensor(dist, dist, bcast(sq[:, tiles], KNN), ALU.add))
                v.tensor_scalar(dist, dist, 0.0, D2_EPS, ALU.max, ALU.add).then_inc(dist_ok, 1)
                v.wait_ge(near_ok, g + 1)
                lk(v.tensor_reduce(tiny[:, 2], near, AX, ALU.add))
                v.tensor_tensor(tiny[:, 0], tiny[:, 2], rowsum[:, tiles], ALU.add).then_inc(r2_ok, 1)
                v.wait_ge(r2_ok, g + 1)
                hold(v)
                v.tensor_copy(sval[:, tiles], near)
                v.tensor_copy(sidx[:, tiles], place[:, :, 0:KNN]).then_inc(dve3, 1)
                lk.n += 1
                v.wait_ge(dve3, lk.base + lk.n)
                v.wait_ge(root2_ok, g + 1)
                newton(lk, tiny[:, 0], tiny[:, 1], tiny[:, 3], tiny[:, 2], d2g)
                hold(v)
                lk(v.tensor_copy(d2s[:, tiles], d2g))
                v.wait_ge(s_xn, 16 * (g + 1))
                if not (isinstance(g, int) and g == 0):
                    v.wait_ge(prodb, 2 * HB * g)
                    v.wait_ge(s_xg, 16 * g)
                v.tensor_tensor(xg, xn, bcast(d2g, D), ALU.mult).then_inc(xg_ok, 1)
                v.wait_ge(xg_ok, g + 1)
                assert lk.n == CH3

            def group_dve(g):
                for j in range(GT):
                    find(g, j)
                chain(g)

            group_dve(0)
            with v.Fori(1, G) as g:
                group_dve(g)

            LK4 = 6 + 2 + 12
            v.wait_ge(added, HB * G)

            def fetch(s, k, first):
                lk = Link(v, dve4, LK4 * s + 3 * k)
                ib = HB + s if k == 0 else s
                if not first:
                    v.wait_ge(gs_ok, 2 * s - 1 + k)
                    v.wait_ge(out_ok, 2 * s - 1 + k)
                hold(v)
                lk(v.tensor_copy(gidx[k], sidx[:, bass.ds(ib * TB, TB)].rearrange("p t m -> p (t m)")))
                hold(v)
                lk(v.tensor_copy(gval[k], sval[:, bass.ds(ib * TB, TB)].rearrange("p t m -> p (t m)")))
                hold(v)
                lk(v.tensor_copy(gd2[k], d2s[:, bass.ds(ib * TB, TB)]))
                v.sem_inc(gi_ok, 1)

            def step_dve(s, first):
                for k in range(2):
                    fetch(s, k, first)
                lk = Link(v, dve4, LK4 * s + 6)
                for k in range(2):
                    v.wait_ge(s_gx[k], 16 * TB * KNN * (s + 1))
                    lk(v.tensor_tensor(gx[k], gx[k], bcast(gval[k], D), ALU.mult))
                    if not first:
                        v.wait_ge(u_ok, 2 * s - 1 + k)
                    v.tensor_reduce(gs[k], gx[k].rearrange("p (j m) d -> p j d m", m=KNN), AX, ALU.add)\
                     .then_inc(gs_ok, 1)
                for k in range(2):
                    if k == 1:
                        v.wait_ge(u_ok, 2 * s + 2)
                        if not first:
                            v.wait_ge(v_ok, 2 * s)
                        v.tensor_tensor(yf[1], PS[:, 1], acc[:, bass.ds(s * BC, BC)], ALU.add).then_inc(yf_ok, 1)
                    v.wait_ge(s_xb[k], 16 * (s + 1))
                    lk(v.tensor_tensor(xb[k], xb[k], b2r[:, :].unsqueeze(1).to_broadcast([P, TB, D]), ALU.add))
                    v.wait_ge(v_ok, 2 * s + k + 1)
                    for j in range(TB):
                        i = v.scalar_tensor_tensor(xb[k][:, j], PS[:, 2 + k, j * P:(j + 1) * P], gd2[k][:, j:j + 1],
                                                   xb[k][:, j], ALU.mult, ALU.add)
                    lk(i)
                    hold(v)
                    for j in range(TB):
                        i = v.bn_stats(stats[:, j], xb[k][:, j])
                    lk(i)
                    hold(v)
                    for j in range(TB):
                        i = v.bn_aggr(mv[:, j], stats[:, j])
                    lk(i)
                    v.tensor_scalar(mv[:, :, 1], mv[:, :, 1], LN_EPS, None, ALU.add).then_inc(var_ok, 1)
                    v.wait_ge(std_ok, 2 * s + k + 1)
                    lk(v.reciprocal(rstd, rstd))
                    if not first:
                        v.wait_ge(s_out[k], 16 * s)
                    for j in range(TB):
                        i = v.tensor_scalar(res[k][:, j], xb[k][:, j], mv[:, j, 0:1], rstd[:, j:j + 1],
                                            ALU.subtract, ALU.mult)
                    lk(i)
                    v.sem_inc(res_free, 1)
                    v.sem_inc(out_ok, 1)
                assert lk.n + 6 == LK4

            step_dve(0, True)
            with v.Fori(1, HB) as s:
                step_dve(s, False)


def kernel(x, adj, L0_gnn_W1, L0_gnn_b1, L0_gnn_W2, L0_gnn_b2):
    import concourse.bacc as bacc
    from concourse.bass_utils import run_bass_kernel_spmd

    adj = np.asarray(adj)
    at = np.ascontiguousarray(adj.reshape(B, BC, T, P).transpose(0, 3, 2, 1))
    arrays = {
        "x": np.ascontiguousarray(x), "at": at,
        "W1": np.ascontiguousarray(L0_gnn_W1), "b1": np.ascontiguousarray(L0_gnn_b1),
        "W2": np.ascontiguousarray(L0_gnn_W2), "b2": np.ascontiguousarray(L0_gnn_b2),
        "consts": constants(),
    }
    nc = bacc.Bacc("TRN2", target_bir_lowering=False, num_devices=1)
    ins = {k: nc.dram_tensor(k, a.shape, F32, kind="ExternalInput").ap() for k, a in arrays.items()}
    out = nc.dram_tensor("out", (N, D), F32, kind="ExternalOutput").ap()
    xs_dram = nc.dram_tensor("xs_dram", (N, D), F32, kind="Internal").ap()
    build(nc, **ins, out=out, xs_dram=xs_dram)
    r = run_bass_kernel_spmd(nc, [arrays], core_ids=[0])
    return r.results[0]["out"]
```

```python
import numpy as np
import concourse.bass as bass
from concourse import mybir
from contextlib import ExitStack

F32 = mybir.dt.float32
F32R = mybir.dt.float32r
U32 = mybir.dt.uint32
ALU = mybir.AluOpType
ACT = mybir.ActivationFunctionType
AX = mybir.AxisListType.X

N, D, P = 8192, 128, 128
T = N // P
BC = 512
B = N // BC
TB = BC // P
KNN, TOP = 4, 8
GT = 8
G = T // GT
HB = 9
HEAVY, LIGHT = 0, 1
EC = 2 * BC
NE = N // EC
SQH = B // 2
SLOTS_A, SLOTS_B = 6, 4
SLOT = TB * BC
PT = 2
PIECE = PT * BC
PIECES = GT // PT
RAW, SPLIT = 3, 2
LN_EPS, D2_EPS, SLOPE = 1e-5, 1e-10, 0.1

C_ID, C_WIN = 0, P
WIN = P + 2 * (SQH - 1)
C_E = C_WIN + WIN
C_MASK = C_E + SQH * P
C_ALL = C_MASK + 2


def constants():
    c = np.zeros((P, C_ALL), np.float32)
    c[:, C_ID:C_ID + P] = np.eye(P)
    c[:, C_WIN + 2 * (SQH - 1):C_WIN + 2 * SQH] = -0.5
    for k in range(SQH):
        c[2 * k:2 * k + 2, C_E + k * P:C_E + (k + 1) * P] = 1.0
    c[0::2, C_MASK] = 1.0
    c[1::2, C_MASK + 1] = 1.0
    return c


def plan_ab():
    one = []
    for b in range(B):
        low = list(range(0, b - b % 2, 2))
        high = list(range(b - b % 2 + 2, B, 2))
        order = []
        while low or high:
            more_high = len(high) * (len(order) + 1) > 0 and len(high) >= len(low)
            order.append((high if more_high else low).pop(0))
        order.append(b - b % 2)
        for q in order:
            one += [(b, q), (b, q + 1)]
    two = [(b, q) for b in reversed(range(B)) for q in range(b + 1, B)]
    return one, two


def build(nc, x, at, W1, b1, W2, b2, consts, out, xs_dram):
    one, two = plan_ab()
    n_one = len(one)
    ctx = ExitStack()
    with ctx:
        top_of = {"next": -(-nc.sbuf_base // 64) * 64}

        def sb(name, shape, dt=F32, at=None):
            if at is None:
                at = top_of["next"]
                top_of["next"] += -(-int(np.prod(shape[1:])) * 4 // 64) * 64
            top_of[name] = at
            return nc.alloc_sbuf_tensor_at(name, shape, dt, offset=at)

        def sem(name):
            return ctx.enter_context(nc.semaphore(name))

        R1 = sb("R1", [P, 2 * N])
        R2 = sb("R2", [P, N])
        ring = sb("ring", [P, SLOTS_B, TB, BC])
        zh = sb("zh", [P, N], F32R)
        zl = sb("zl", [P, N], F32R)
        sqn = sb("sqn", [P, 2, BC], F32R)
        sel = sb("sel", [P, SQH, P], F32R)
        zst = sb("zst", [P, 2, 2, P], F32R)
        ident = sb("ident", [P, P])
        w1 = sb("w1", [P, D])
        w2 = sb("w2", [P, D])
        b1r = sb("b1r", [P, D])
        b2r = sb("b2r", [P, D])
        masks = sb("masks", [P, 2])
        ones = sb("ones", [P, 1])
        rowsum = sb("rowsum", [P, T])
        dsc = sb("dsc", [P, T])
        sq = sb("sq", [P, T])
        d2s = sb("d2s", [P, T])
        sval_t = sb("sval_t", [P, T * KNN])
        tiny = sb("tiny", [P, 5, GT])

        xs = R1[:, 0:N].rearrange("p (t d) -> p t d", d=D)
        pairs = [ring[:, 0:2].rearrange("p s k c -> p (s k) c"), ring[:, 2:4].rearrange("p s k c -> p (s k) c"),
                 R1[:, N:N + 2 * SLOT].rearrange("p (k c) -> p k c", c=BC)]
        slots_a = [pairs[s // 2][:, s % 2 * TB:(s % 2 + 1) * TB] for s in range(SLOTS_A)]
        tmp = R1[:, 2 * N - SLOT:2 * N]
        part = [tmp[:, 0:BC], tmp[:, BC:2 * BC]]
        e_raw = tmp[:, 0:SQH * P]
        y = tmp[:, 0:BC]
        zn = tmp[:, BC:2 * BC].rearrange("p (j d) -> p j d", j=TB)
        window = tmp[:, 2 * BC:2 * BC + WIN]
        junk = tmp[:, 2 * BC + 256:2 * BC + 256 + P]
        z2 = tmp[:, 3 * BC:4 * BC]
        score = [R1[:, 0:N], R1[:, N:2 * N]]
        raw = [ring[:, :].rearrange("p s k c -> p (s k c)")[:, i * PIECE:(i + 1) * PIECE]
               .rearrange("p (k c) -> p k c", k=PT) for i in range(RAW)]
        over = top_of["ring"] + RAW * PIECE * 4
        ah = sb("ah", [P, SPLIT, PT, BC], F32R, at=over)
        al = sb("al", [P, SPLIT, PT, BC], F32R, at=over + SPLIT * PIECE * 4)
        xgh = sb("xgh", [P, GT, D], F32R, at=over + 2 * SPLIT * PIECE * 4)
        acc = R2[:, 0:HB * BC]
        at_ = [HB * BC]

        def cut(n):
            at_[0] += n
            return R2[:, at_[0] - n:at_[0]]

        xg = cut(GT * D).rearrange("p (j d) -> p j d", j=GT)
        flush = cut(BC)
        top = cut(GT * TOP).rearrange("p (j m) -> p j m", j=GT)
        place = cut(GT * TOP).bitcast(U32).rearrange("p (j m) -> p j m", j=GT)
        dist = cut(GT * KNN).rearrange("p (j m) -> p j m", j=GT)
        near = cut(GT * KNN).rearrange("p (j m) -> p j m", j=GT)
        sval = sval_t[:, :].rearrange("p (t m) -> p t m", t=T)
        sidx = cut(T * KNN).bitcast(U32).rearrange("p (t m) -> p t m", t=T)
        assert at_[0] + GT * D <= N
        xgl = sb("xgl", [P, GT, D], F32R, at=top_of["R2"] + 4 * at_[0])
        xsc = R1[:, 0:N].rearrange("p (t d) -> p t d", d=D)
        bt = [N]

        def cut1(n):
            bt[0] += n
            return R1[:, bt[0] - n:bt[0]]

        gx = [cut1(TB * KNN * D).rearrange("p (j m d) -> p (j m) d", j=TB, m=KNN) for _ in range(2)]
        gs = [cut1(BC).rearrange("p (j d) -> p j d", j=TB) for _ in range(2)]
        yf = [cut1(BC) for _ in range(2)]
        xb = [cut1(BC).rearrange("p (j d) -> p j d", j=TB) for _ in range(2)]
        res = [cut1(BC).rearrange("p (j d) -> p j d", j=TB) for _ in range(2)]
        small = sb("small", [P, 2 * TB * (2 * KNN + 1 + 6 + 2 + 1)])
        ct = [0]

        def cut2(n):
            ct[0] += n
            return small[:, ct[0] - n:ct[0]]

        gidx = [cut2(TB * KNN).bitcast(U32) for _ in range(2)]
        gval = [cut2(TB * KNN) for _ in range(2)]
        gd2 = [cut2(TB) for _ in range(2)]
        stats = [cut2(TB * 6).rearrange("p (j s) -> p j s", j=TB) for _ in range(2)]
        mv = [cut2(TB * 2).rearrange("p (j s) -> p j s", j=TB) for _ in range(2)]
        rstd = [cut2(TB) for _ in range(2)]

        PS = ctx.enter_context(nc.psum_tensor("PS", [P, 8, BC], F32))

        gate = sem("gate")
        s_const = sem("s_const")
        s_x = sem("s_x")
        ld_a = [sem(f"ld_a{s}") for s in range(SLOTS_A)]
        const_ok = sem("const_ok")
        reduced = sem("reduced")
        summed = sem("summed")
        diag_done = sem("diag_done")
        sums_read = sem("sums_read")
        root_ok = sem("root_ok")
        xs_ok = sem("xs_ok")
        y_saved = sem("y_saved")
        prod2 = sem("prod2")
        y_ok = sem("y_ok")
        zraw = sem("zraw")
        zn_ok = sem("zn_ok")
        sq_ok = sem("sq_ok")
        zt = sem("zt")
        z2_ok = sem("z2_ok")
        zl_ok = sem("zl_ok")
        sqs = sem("sqs")
        sqn_ok = sem("sqn_ok")
        dve = sem("dve")
        dve3 = sem("dve3")
        dve4 = sem("dve4")
        act1 = sem("act1")
        st_ok = sem("st_ok")
        gram = sem("gram")
        copied = sem("copied")
        placed = sem("placed")
        dist_ok = sem("dist_ok")
        near_ok = sem("near_ok")
        act3 = sem("act3")
        r2_ok = sem("r2_ok")
        root2_ok = sem("root2_ok")
        s_xn = sem("s_xn")
        xg_ok = sem("xg_ok")
        s_xg = sem("s_xg")
        acc0 = sem("acc0")
        ld_b = [sem(f"ld_b{s}") for s in range(RAW)]
        prodb = sem("prodb")
        flushed = sem("flushed")
        added = sem("added")
        s_xsc = sem("s_xsc")
        ld_c = [sem(f"ld_c{s}") for s in range(SLOTS_B)]
        prod4 = sem("prod4")
        rounded = sem("rounded")
        rest = sem("rest")
        idx_ok = sem("idx_ok")
        xgh_ok = sem("xgh_ok")

        def pair(name):
            return [sem(f"{name}_{k}") for k in ("heavy", "light")]

        dve4, fin = pair("dve4"), pair("fin")
        gi_ok = pair("gi_ok")
        s_gx = pair("s_gx")
        wt_ok = pair("wt_ok")
        gs_ok = pair("gs_ok")
        u_ok = pair("u_ok")
        yf_ok = pair("yf_ok")
        v_ok = pair("v_ok")
        s_xb = pair("s_xb")
        var_ok = pair("var_ok")
        std_ok = pair("std_ok")
        out_ok = pair("out_ok")
        s_out = pair("s_out")

        block = ctx.enter_context(nc.Block())

        class Link:
            def __init__(self, eng, own, base):
                self.eng, self.own, self.base, self.n = eng, own, base, 0

            def __call__(self, ins):
                self.n += 1
                ins.then_inc(self.own, 1)
                self.eng.wait_ge(self.own, self.base + self.n)

        def hold(eng):
            eng.sem_inc(gate, 1)

        def bcast(ap, n):
            return ap.unsqueeze(len(ap.shape)).to_broadcast(list(ap.shape) + [n])

        def newton(link, r, root, y0, a, y1):
            link(nc.vector.reciprocal(y0, root))
            link(nc.vector.tensor_tensor(a, y0, y0, ALU.mult))
            link(nc.vector.tensor_tensor(a, a, r, ALU.mult))
            link(nc.vector.tensor_scalar(a, a, -0.5, 1.5, ALU.mult, ALU.add))
            link(nc.vector.tensor_tensor(y1, y0, a, ALU.mult))

        blocks2 = list(reversed(range(B)))
        last_quad = {}
        for n, (b, q) in enumerate(two):
            last_quad[b] = n + 1
        CHA, CHB = 2, 9

        TWO = HB - (B - HB)

        def is_first(n):
            return isinstance(n, int) and n == 0

        def lights(s):
            return [2 * s, 2 * s + 1] if isinstance(s, int) and s < TWO else [s + TWO]

        LATE, NP = 2, HB * PIECES
        early, late = (HB - LATE) * PIECES, LATE * PIECES
        turn = [[[] for _ in range(NE)] for _ in range(GT)]
        for k in range(late):
            at_k = (2 * k + 1) * NE // late
            turn[at_k // NE][at_k % NE].append((2, early + k))
        for k in range(early):
            at_k = 2 * NE + ((k + 1) * (GT - 2) * NE - 1) // early
            turn[at_k // NE][at_k % NE].append((1, k))

        @block.sync
        def _(sp):
            sp.dma_start(ident[:, :], consts[:, C_ID:C_ID + P]).then_inc(s_const, 16)
            sp.dma_start(e_raw, consts[:, C_E:C_E + SQH * P]).then_inc(s_const, 16)
            sp.dma_start(window, consts[:, C_WIN:C_WIN + WIN]).then_inc(s_const, 16)
            sp.dma_start(masks[:, :], consts[:, C_MASK:C_MASK + 2]).then_inc(s_const, 16)
            sp.dma_start(w1[:, :], W1).then_inc(s_const, 16)
            sp.dma_start(w2[:, :], W2).then_inc(s_const, 16)
            sp.dma_start(b1r[:, :], b1.partition_broadcast(P)).then_inc(s_const, 16)
            sp.dma_start(b2r[:, :], b2.partition_broadcast(P)).then_inc(s_const, 16)
            for n, (b, q) in enumerate(one + two):
                m = n - SLOTS_A
                if m >= n_one:
                    sp.wait_ge(prod2, m - n_one + 1)
                elif m >= 0:
                    sp.wait_ge(summed, m // 2 + 1)
                    if m % B >= B - 2:
                        sp.wait_ge(diag_done, m // B + 1)
                sp.dma_start(slots_a[n % SLOTS_A], at[b, :, q * TB:(q + 1) * TB, :])\
                  .then_inc(ld_a[n % SLOTS_A], 16)
                if n == 1:
                    sp.dma_start(xs, x.rearrange("(t p) d -> p t d", p=P)).then_inc(s_x, 16)

            sp.wait_ge(prod2, len(two))
            sp.wait_ge(y_ok, B)
            sp.dma_start(xg, x[0:GT * P].rearrange("(t p) d -> p t d", p=P)).then_inc(s_xn, 16)

            def group_loads(g, first):
                for k in range(NP):
                    ib, p = k // PIECES, k % PIECES
                    if not first or k >= RAW:
                        sp.wait_ge(rest, g * NP + (k - RAW + 1))
                    src = at[ib, :, bass.ds(g * GT + p * PT, PT), :]
                    sp.dma_start(raw[k % RAW], src).then_inc(ld_b[k % RAW], 16)
                    if k == RAW - 1:
                        sp.wait_ge(xg_ok, g + 1)
                        dst = xs_dram[bass.ds(g * GT * P, GT * P)]
                        sp.dma_start(dst.rearrange("(t p) d -> p t d", p=P), xg).then_inc(s_xg, 16)
                        if not (isinstance(g, int) and g == G - 1):
                            sp.wait_ge(s_xg, 16 * (g + 1))
                            src = x[bass.ds((g + 1) * GT * P, GT * P)]
                            sp.dma_start(xg, src.rearrange("(t p) d -> p t d", p=P)).then_inc(s_xn, 16)

            group_loads(0, True)
            with sp.Fori(1, G - 1) as g:
                group_loads(g, False)
            group_loads(G - 1, False)

            sp.wait_ge(s_xg, 16 * G)
            sp.wait_ge(placed, T)
            sp.dma_start(xsc, xs_dram.rearrange("(t p) d -> p t d", p=P)).then_inc(s_xsc, 16)
            sp.wait_ge(prodb, G * NP)

            def step_loads(s, first):
                for h in range(B):
                    slot = h % SLOTS_B
                    if not first or h >= SLOTS_B:
                        sp.wait_ge(prod4, s * B + (h - SLOTS_B + 1))
                    src = at[bass.ds(HB + s, 1), :, h * TB:(h + 1) * TB, :]
                    sp.dma_start(ring[:, slot], src.rearrange("o p k c -> p (o k) c")).then_inc(ld_c[slot], 16)

            step_loads(0, True)
            with sp.Fori(1, B - HB) as s:
                step_loads(s, False)

        @block.tensor
        def _(pe):
            pe.wait_ge(const_ok, 1)
            started = [0] * B
            for m in range(n_one // 2):
                b = one[2 * m][0]
                prod, sums = PS[:, b % 2], PS[:, 2 + b % 2]
                first_pair, last_pair = 2 * m % B == 0, 2 * m % B == B - 2

                def products(n, q):
                    pe.wait_ge(ld_a[n % SLOTS_A], 16 * (n // SLOTS_A + 1))
                    pe.wait_ge(xs_ok, q + 1)
                    start = started[b] == 0
                    started[b] += 1
                    if start and b >= 2:
                        pe.wait_ge(y_saved, b - 1)
                    for k in range(TB):
                        i = pe.matmul(prod, xs[:, q * TB + k], slots_a[n % SLOTS_A][:, k], start=start and k == 0,
                                      stop=q == b and k == TB - 1)
                    return i

                for n in (2 * m, 2 * m + 1):
                    if one[n][1] < b:
                        products(n, one[n][1])
                pe.wait_ge(reduced, m + 1)
                if first_pair and b >= 2:
                    pe.wait_ge(sums_read, b - 1)
                for j in range(TB):
                    i = pe.matmul(sums[:, j:j + 1], part[m % 2][:, j * P:(j + 1) * P], ones[:, :],
                                  start=first_pair and j == 0, stop=last_pair and j == TB - 1,
                                  skip_group_check=True)
                i.then_inc(summed, 1)
                if last_pair:
                    n = 2 * m + (one[2 * m][1] != b)
                    products(n, b).then_inc(diag_done, 1)

            def z_raw(pi):
                b = blocks2[pi]
                pe.wait_ge(y_ok, pi + 1)
                if pi >= 1:
                    pe.wait_ge(zn_ok, pi)
                for j in range(TB):
                    i = pe.matmul(PS[:, 4, j * P:(j + 1) * P], y[:, j * P:(j + 1) * P], w1[:, :],
                                  start=True, stop=True)
                i.then_inc(zraw, 1)

            def z_transposed(pi):
                pe.wait_ge(zn_ok, pi + 1)
                if pi >= 1:
                    pe.wait_ge(zl_ok, pi)
                    pe.wait_ge(z2_ok, pi)
                for j in range(TB):
                    i = pe.transpose(PS[:, 5, j * P:(j + 1) * P], zn[:, j], ident[:, :])
                i.then_inc(zt, 1)

            def squares(pi):
                b = blocks2[pi]
                k = b % SQH
                pe.wait_ge(z2_ok, pi + 1)
                pe.matmul(PS[:, 6 + b // SQH], window[:, 2 * (SQH - 1 - k):2 * (SQH - 1 - k) + P], z2,
                          start=k == SQH - 1, stop=k == 0).then_inc(sqs, 1)

            n = n_one
            for pi, b in enumerate(blocks2):
                prod = PS[:, pi % 2]
                if pi >= 1:
                    if pi >= 3:
                        pe.wait_ge(y_ok, pi - 1)
                    else:
                        pe.wait_ge(y_saved, B)
                for q in range(b + 1, B):
                    pe.wait_ge(ld_a[n % SLOTS_A], 16 * (n // SLOTS_A + 1))
                    for k in range(TB):
                        i = pe.matmul(prod, xs[:, q * TB + k], slots_a[n % SLOTS_A][:, k],
                                      start=q == b + 1 and k == 0, stop=q == B - 1 and k == TB - 1)
                    i.then_inc(prod2, 1)
                    n += 1
                if pi >= 1:
                    z_raw(pi - 1)
                if pi >= 2:
                    z_transposed(pi - 2)
                if pi >= 3:
                    squares(pi - 3)
            z_raw(B - 1)
            z_transposed(B - 2)
            squares(B - 3)
            z_transposed(B - 1)
            squares(B - 2)
            squares(B - 1)

            def scores(g, j, c, first):
                par = j % 2
                if c == 0:
                    pe.wait_ge(st_ok, 2 * (GT * g + j) + 2)
                if not (first and j == 0 and c < 2):
                    pe.wait_ge(copied, NE * (GT * g + j) + c - 1)
                for h in range(2):
                    cc = 2 * c + h
                    bank = PS[:, 2 * (c % 2) + h]
                    cols = slice(cc * BC, (cc + 1) * BC)
                    pe.matmul(bank, zst[:, par, 0], zh[:, cols], start=True, stop=False)
                    pe.matmul(bank, zst[:, par, 0], zl[:, cols], start=False, stop=False)
                    pe.matmul(bank, zst[:, par, 1], zh[:, cols], start=False, stop=False)
                    i = pe.matmul(bank, sel[:, cc % SQH], sqn[:, cc // SQH], start=False, stop=True)
                i.then_inc(gram, 1)

            def piece(g, k):
                ib, p, s = k // PIECES, k % PIECES, k % SPLIT
                bank = PS[:, 4 + ib % 3]
                if p == 0:
                    if not (isinstance(g, int) and g == 0 and ib < 3):
                        pe.wait_ge(flushed, HB * g + ib - 2)
                    if ib == 0:
                        pe.wait_ge(xg_ok, g + 1)
                pe.wait_ge(rounded, NP * g + k + 1)
                for kk in range(PT):
                    t = p * PT + kk
                    pe.matmul(bank, xgh[:, t], ah[:, s, kk], start=p == 0 and kk == 0, stop=False)
                    pe.matmul(bank, xgl[:, t], ah[:, s, kk], start=False, stop=False)
                pe.wait_ge(rest, NP * g + k + 1)
                for kk in range(PT):
                    i = pe.matmul(bank, xgh[:, p * PT + kk], al[:, s, kk], start=False,
                                  stop=p == PIECES - 1 and kk == PT - 1)
                i.then_inc(prodb, 1)

            def group_pe(g):
                for j in range(GT):
                    for c in range(NE):
                        scores(g, j, c, isinstance(g, int) and g == 0)
                        for back, k in turn[j][c]:
                            if not isinstance(g, int) or g >= back:
                                piece(g - back, k)

            pe.wait_ge(sqn_ok, 1)
            for g in (0, 1, 2):
                group_pe(g)
            with pe.Fori(3, G) as g:
                group_pe(g)
            for k in range(early, NP):
                piece(G - 2, k)
            for k in range(NP):
                piece(G - 1, k)

            pe.wait_ge(s_xsc, 16)
            pe.wait_ge(flushed, HB * G)

            def quads(s, hs):
                for h in hs:
                    slot = h % SLOTS_B
                    pe.wait_ge(ld_c[slot], 16 * ((B // SLOTS_B) * s + h // SLOTS_B + 1))
                    if h == 0 and not is_first(s):
                        pe.wait_ge(yf_ok[HEAVY], s)
                    for kk in range(TB):
                        i = pe.matmul(PS[:, HEAVY], xsc[:, h * TB + kk], ring[:, slot, kk],
                                      start=h == 0 and kk == 0, stop=h == B - 1 and kk == TB - 1)
                    i.then_inc(prod4, 1)

            def gathered(k, n):
                if k == LIGHT and not is_first(n):
                    pe.wait_ge(yf_ok[k], n)
                pe.wait_ge(gs_ok[k], n + 1)
                for j in range(TB):
                    i = pe.matmul(PS[:, k, j * P:(j + 1) * P], gs[k][:, j], ident[:, :],
                                  start=k == LIGHT, stop=True, skip_group_check=True)
                i.then_inc(u_ok[k], 1)

            def times_w2(k, n):
                pe.wait_ge(yf_ok[k], n + 1)
                if not is_first(n):
                    pe.wait_ge(var_ok[k], n)
                for j in range(TB):
                    i = pe.matmul(PS[:, 2 + k, j * P:(j + 1) * P], yf[k][:, j * P:(j + 1) * P], w2[:, :],
                                  start=True, stop=True)
                i.then_inc(v_ok[k], 1)

            def step_pe(s):
                ls = lights(s)
                quads(s, [0, 1])
                if not is_first(s):
                    times_w2(HEAVY, s - 1)
                quads(s, [2, 3, 4])
                gathered(LIGHT, ls[0])
                quads(s, [5, 6])
                times_w2(LIGHT, ls[0])
                quads(s, [7, 8, 9, 10, 11])
                if len(ls) > 1:
                    gathered(LIGHT, ls[1])
                    quads(s, [12, 13])
                    times_w2(LIGHT, ls[1])
                    quads(s, [14, 15])
                else:
                    quads(s, [12, 13, 14, 15])
                gathered(HEAVY, s)

            for s in range(TWO):
                step_pe(s)
            with pe.Fori(TWO, B - HB) as s:
                step_pe(s)
            times_w2(HEAVY, B - HB - 1)

        @block.scalar
        def _(act):
            for b in range(B):
                act.wait_ge(sums_read, b + 1)
                act.activation(tiny[:, 0, 0:TB], rowsum[:, b * TB:(b + 1) * TB], ACT.Sqrt).then_inc(root_ok, 1)
                act.wait_ge(diag_done, b + 1)
                act.activation(R2[:, b * BC:(b + 1) * BC], PS[:, b % 2], ACT.Copy).then_inc(y_saved, 1)
                if b < B - 1:
                    act.wait_ge(xs_ok, b + 1)

            def z_squares(pi):
                b = blocks2[pi]
                act.wait_ge(zn_ok, pi + 1)
                for j in range(TB):
                    if pi + j:
                        act.wait_ge(sq_ok, TB * pi + j)
                    act.activation(junk, zn[:, j], ACT.Square,
                                   accum_out=sq[:, b * TB + j:b * TB + j + 1]).then_inc(sq_ok, 1)

            def z_split(pi):
                b = blocks2[pi]
                act.wait_ge(zt, pi + 1)
                act.activation(zh[:, b * BC:(b + 1) * BC], PS[:, 5], ACT.Copy)
                if pi >= 1:
                    act.wait_ge(sqs, pi)
                act.activation(z2, PS[:, 5], ACT.Square).then_inc(z2_ok, 1)

            for pi in range(B):
                z_squares(pi)
                z_split(pi)

            def s_of_distances(g):
                act.wait_ge(dist_ok, g + 1)
                act.activation(dist, dist, ACT.Sqrt).then_inc(act3, 1)
                act.wait_ge(act3, g + 1)
                act.activation(near, dist, ACT.Exp, scale=-0.5).then_inc(near_ok, 1)

            def root_of_sums(g):
                act.wait_ge(r2_ok, g + 1)
                act.activation(tiny[:, 1], tiny[:, 0], ACT.Sqrt).then_inc(root2_ok, 1)

            def round_piece(g, k):
                turns = (NP // RAW) * g + k // RAW + 1
                n, k = NP * g + k, k % NP
                act.wait_ge(ld_b[k % RAW], 16 * turns)
                if not (isinstance(g, int) and n < SPLIT):
                    act.wait_ge(prodb, n - SPLIT + 1)
                act.activation(ah[:, k % SPLIT], raw[k % RAW], ACT.Copy).then_inc(rounded, 1)

            def flush_unit(g, ib):
                act.wait_ge(prodb, PIECES * (HB * g + ib + 1))
                if not (isinstance(g, int) and g == 0 and ib == 0):
                    act.wait_ge(added, HB * g + ib)
                act.activation(flush, PS[:, 4 + ib % 3], ACT.Copy).then_inc(flushed, 1)

            def group_act(g):
                first = isinstance(g, int) and g == 0
                for j in range(GT):
                    for c in range(NE):
                        if c == 0 and not (first and j < 2):
                            act.wait_ge(placed, GT * g + j - 1)
                        if c == 0 and first and j == 0:
                            act.wait_ge(prod2, len(two))
                            act.wait_ge(sqs, B)
                        act.wait_ge(gram, NE * (GT * g + j) + c + 1)
                        act.activation(score[j % 2][:, c * EC:(c + 1) * EC],
                                       PS[:, 2 * (c % 2):2 * (c % 2) + 2].rearrange("p b c -> p (b c)"),
                                       ACT.Copy).then_inc(copied, 1)
                        if not first and (j, c) == (1, 1):
                            s_of_distances(g - 1)
                        if not first and (j, c) == (2, 0):
                            root_of_sums(g - 1)
                        for back, k in turn[j][c]:
                            if not isinstance(g, int) or g >= back:
                                round_piece(g - back, k + 1)
                                if k % PIECES == 0 and not (isinstance(g, int) and g == back and k == 0):
                                    flush_unit(*((g - back, k // PIECES - 1) if k else (g - back - 1, HB - 1)))

            group_act(0)
            round_piece(0, 0)
            for g in (1, 2):
                group_act(g)
            with act.Fori(3, G) as g:
                group_act(g)
            for k in range(early, NP):
                round_piece(G - 2, k + 1)
                if k % PIECES == 0:
                    flush_unit(G - 2, k // PIECES - 1)
            s_of_distances(G - 1)
            root_of_sums(G - 1)
            for k in range(NP):
                if k + 1 < NP:
                    round_piece(G - 1, k + 1)
                if k % PIECES == 0:
                    flush_unit(*((G - 1, k // PIECES - 1) if k else (G - 2, HB - 1)))
            flush_unit(G - 1, HB - 1)

            def block_io(k, n, row):
                if not is_first(n):
                    act.wait_ge(out_ok[k], n)
                act.dma_start(xb[k], x[bass.ds(row, BC)].rearrange("(t p) d -> p t d", p=P)).then_inc(s_xb[k], 16)
                if k == HEAVY:
                    act.wait_ge(u_ok[k], n + 1)
                    if not is_first(n):
                        act.wait_ge(v_ok[k], n)
                    act.activation(yf[k], PS[:, k], ACT.Copy).then_inc(yf_ok[k], 1)
                act.wait_ge(var_ok[k], n + 1)
                act.activation(rstd[k], mv[k][:, :, 1], ACT.Sqrt).then_inc(std_ok[k], 1)
                act.wait_ge(out_ok[k], n + 1)
                act.dma_start(out[bass.ds(row, BC)].rearrange("(t p) d -> p t d", p=P), res[k])\
                   .then_inc(s_out[k], 16)

            def step_act(s):
                for l in lights(s):
                    block_io(LIGHT, l, l * BC)
                block_io(HEAVY, s, (HB + s) * BC)

            for s in range(TWO):
                step_act(s)
            with act.Fori(TWO, B - HB) as s:
                step_act(s)
            act.wait_ge(s_out[HEAVY], 16 * (B - HB))
            act.wait_ge(s_out[LIGHT], 16 * HB)

        @block.gpsimd
        def _(pool):
            def stationary(g, j, first):
                if not (first and j < 2):
                    pool.wait_ge(gram, NE * (GT * g + j - 1))
                    hold(pool)
                t = (GT * g + j) * P
                pool.tensor_copy(zst[:, j % 2, 0], zh[:, bass.ds(t, P)]).then_inc(st_ok, 1)
                pool.tensor_copy(zst[:, j % 2, 1], zl[:, bass.ds(t, P)]).then_inc(st_ok, 1)

            def add_unit(g, ib):
                pool.wait_ge(flushed, HB * g + ib + 1)
                cols = acc[:, ib * BC:(ib + 1) * BC]
                pool.tensor_tensor(cols, cols, flush, ALU.add).then_inc(added, 1)

            def rest_of_piece(g, k):
                n, k = NP * g + k, k % NP
                pool.wait_ge(rounded, n + 1)
                pool.tensor_tensor(al[:, k % SPLIT], raw[k % RAW], ah[:, k % SPLIT].bitcast(F32), ALU.subtract)\
                    .then_inc(rest, 1)

            def group_pool(g):
                first = isinstance(g, int) and g == 0
                for j in range(GT):
                    if j < GT - 1:
                        stationary(g, j + 1, first)
                    elif not (isinstance(g, int) and g == G - 1):
                        stationary(g + 1, 0, False)
                    for c in range(NE):
                        for back, k in turn[j][c]:
                            if not isinstance(g, int) or g >= back:
                                rest_of_piece(g - back, k + 1)
                                if k % PIECES == 0 and not (isinstance(g, int) and g == back and k == 0):
                                    add_unit(*((g - back, k // PIECES - 1) if k else (g - back - 1, HB - 1)))

            pool.wait_ge(z2_ok, B)
            pool.wait_ge(zl_ok, B)
            stationary(0, 0, True)
            pool.wait_ge(acc0, 1)
            group_pool(0)
            rest_of_piece(0, 0)
            for g in (1, 2):
                group_pool(g)
            with pool.Fori(3, G - 1) as g:
                group_pool(g)
            group_pool(G - 1)
            for k in range(early, NP):
                rest_of_piece(G - 2, k + 1)
                if k % PIECES == 0:
                    add_unit(G - 2, k // PIECES - 1)
            for k in range(NP):
                if k + 1 < NP:
                    rest_of_piece(G - 1, k + 1)
                if k % PIECES == 0:
                    add_unit(*((G - 1, k // PIECES - 1) if k else (G - 2, HB - 1)))
            add_unit(G - 1, HB - 1)

            pool.wait_ge(s_xg, 16 * G)

            def gather(k, n):
                pool.wait_ge(gi_ok[k], n + 1)
                hold(pool)
                for i in range(TB * KNN):
                    pool.indirect_dma_start(
                        gx[k][:, i], None, xs_dram,
                        bass.IndirectOffsetOnAxis(ap=gidx[k][:, i:i + 1], axis=0)).then_inc(s_gx[k], 16)

            gather(LIGHT, 0)
            gather(HEAVY, 0)

            def step_gathers(s):
                for l in lights(s):
                    if not (isinstance(l, int) and l == HB - 1):
                        gather(LIGHT, l + 1)
                if not (isinstance(s, int) and s == B - HB - 1):
                    gather(HEAVY, s + 1)

            for s in range(TWO):
                step_gathers(s)
            with pool.Fori(TWO, B - HB - 1) as s:
                step_gathers(s)

        @block.vector
        def _(v):
            link = Link(v, dve, 0)
            v.memset(ones[:, :], 1.0).then_inc(dve, 1)
            link.n += 1
            v.wait_ge(s_const, 16 * 8)
            link(v.tensor_copy(sel[:, :, :].rearrange("p k m -> p (k m)"), e_raw))
            v.sem_inc(const_ok, 1)
            v.wait_ge(s_x, 16)

            for m in range(n_one // 2):
                b = one[2 * m][0]
                if m >= 2:
                    v.wait_ge(summed, m - 1)
                for n in (2 * m, 2 * m + 1):
                    v.wait_ge(ld_a[n % SLOTS_A], 16 * (n // SLOTS_A + 1))
                v.tensor_reduce(part[m % 2], pairs[m % 3].rearrange("p k c -> p c k"), AX, ALU.add)\
                 .then_inc(reduced, 1)
                if 2 * m % B != B - 2:
                    continue
                v.wait_ge(summed, m + 1)
                cols = slice(b * TB, (b + 1) * TB)
                v.tensor_copy(rowsum[:, cols], PS[:, 2 + b % 2, 0:TB]).then_inc(sums_read, 1)
                v.wait_ge(sums_read, b + 1)
                v.wait_ge(root_ok, b + 1)
                newton(link, rowsum[:, cols], tiny[:, 0, 0:TB], tiny[:, 1, 0:TB], tiny[:, 2, 0:TB], dsc[:, cols])
                v.tensor_tensor(xs[:, cols], xs[:, cols], bcast(dsc[:, cols], D), ALU.mult).then_inc(xs_ok, 1)

            def make_y(pi):
                b = blocks2[pi]
                v.wait_ge(y_saved, B if b == B - 1 else B)
                if pi == 0:
                    v.wait_ge(summed, n_one // 2)
                else:
                    v.wait_ge(zraw, pi)
                cols = R2[:, b * BC:(b + 1) * BC]
                if b == B - 1:
                    v.tensor_copy(y, cols).then_inc(y_ok, 1)
                else:
                    v.wait_ge(prod2, last_quad[b])
                    v.tensor_tensor(y, cols, PS[:, pi % 2], ALU.add).then_inc(y_ok, 1)

            def make_z(pi):
                b = blocks2[pi]
                v.wait_ge(zraw, pi + 1)
                if pi >= 1:
                    v.wait_ge(zt, pi)
                    v.wait_ge(sq_ok, TB * pi)
                for j in range(TB):
                    t = b * TB + j
                    i = v.scalar_tensor_tensor(zn[:, j], PS[:, 4, j * P:(j + 1) * P], dsc[:, t:t + 1], b1r[:, :],
                                               ALU.mult, ALU.add)
                link(i)
                v.scalar_tensor_tensor(zn, zn, SLOPE, zn, ALU.mult, ALU.max).then_inc(zn_ok, 1)

            def make_zl(pi):
                b = blocks2[pi]
                cols = slice(b * BC, (b + 1) * BC)
                v.wait_ge(z2_ok, pi + 1)
                v.tensor_tensor(zl[:, cols], PS[:, 5], zh[:, cols].bitcast(F32), ALU.subtract).then_inc(zl_ok, 1)

            for pi in range(B):
                make_y(pi)
                if pi >= 1:
                    make_zl(pi - 1)
                make_z(pi)
            make_zl(B - 1)
            v.wait_ge(y_ok, B)
            v.memset(acc, 0.0).then_inc(acc0, 1)
            v.wait_ge(sqs, B)
            for h in range(2):
                hi = tmp[:, h * BC:(h + 1) * BC]
                link(v.tensor_copy(sqn[:, h], PS[:, 6 + h]))
                link(v.tensor_tensor(hi, PS[:, 6 + h], sqn[:, h].bitcast(F32), ALU.subtract))
                link(v.tensor_scalar(hi, hi, masks[:, 1:2], None, ALU.mult))
                link(v.scalar_tensor_tensor(sqn[:, h], sqn[:, h].bitcast(F32), masks[:, 0:1], hi, ALU.mult, ALU.add))
            v.sem_inc(sqn_ok, 1)

            K3 = GT + CHA + CHB

            def base3(g):
                return K3 * g - (0 if is_first(g) else CHA + CHB)

            def find(g, j):
                before = 0 if is_first(g) else CHA if j == 0 else CHA + CHB
                v.wait_ge(copied, NE * (GT * g + j + 1))
                hold(v)
                v.max(top[:, j], score[j % 2]).then_inc(dve3, 1)
                v.wait_ge(dve3, base3(g) + before + j + 1)
                hold(v)
                v.max_index(place[:, j], top[:, j], score[j % 2]).then_inc(placed, 1)

            def chain_a(g):
                lk = Link(v, dve3, base3(g + 1))
                v.wait_ge(placed, GT * (g + 1))
                lk(v.tensor_scalar(dist, top[:, :, 0:KNN], -2.0, None, ALU.mult))
                lk(v.tensor_tensor(dist, dist, bcast(sq[:, bass.ds(g * GT, GT)], KNN), ALU.add))
                assert lk.n == CHA
                v.tensor_scalar(dist, dist, 0.0, D2_EPS, ALU.max, ALU.add).then_inc(dist_ok, 1)
                hold(v)
                v.tensor_copy(sidx[:, bass.ds(g * GT, GT)], place[:, :, 0:KNN]).then_inc(idx_ok, 1)
                v.wait_ge(idx_ok, g + 1)
                hold(v)

            def chain_b(g, behind):
                lk = Link(v, dve3, base3(g + 1) + CHA + behind)
                tiles, d2g = bass.ds(g * GT, GT), tiny[:, 4]
                v.wait_ge(near_ok, g + 1)
                lk(v.tensor_reduce(tiny[:, 2], near, AX, ALU.add))
                v.tensor_tensor(tiny[:, 0], tiny[:, 2], rowsum[:, tiles], ALU.add).then_inc(r2_ok, 1)
                v.wait_ge(r2_ok, g + 1)
                hold(v)
                lk(v.tensor_copy(sval[:, tiles], near))
                v.wait_ge(root2_ok, g + 1)
                newton(lk, tiny[:, 0], tiny[:, 1], tiny[:, 3], tiny[:, 2], d2g)
                hold(v)
                lk(v.tensor_copy(d2s[:, tiles], d2g))
                v.wait_ge(s_xn, 16 * (g + 1))
                lk(v.tensor_tensor(xg, xg, bcast(d2g, D), ALU.mult))
                if not is_first(g):
                    v.wait_ge(prodb, NP * g)
                v.tensor_copy(xgh[:, :, :], xg).then_inc(xgh_ok, 1)
                v.wait_ge(xgh_ok, g + 1)
                v.tensor_tensor(xgl[:, :, :], xg, xgh[:, :, :].bitcast(F32), ALU.subtract).then_inc(xg_ok, 1)
                assert lk.n == CHB

            def group_dve(g):
                if not is_first(g):
                    chain_a(g - 1)
                find(g, 0)
                if not is_first(g):
                    chain_b(g - 1, 1)
                for j in range(1, GT):
                    find(g, j)

            group_dve(0)
            with v.Fori(1, G) as g:
                group_dve(g)
            chain_a(G - 1)
            chain_b(G - 1, 0)

            LKF, LKD = 2, 7
            v.wait_ge(added, HB * G)

            def fetch(k, n):
                lk = Link(v, dve4[k], LKF * n)
                tiles = bass.ds(((HB + n) if k == HEAVY else n) * TB, TB)
                if not is_first(n):
                    v.wait_ge(gs_ok[k], n)
                hold(v)
                lk(v.tensor_copy(gidx[k], sidx[:, tiles].rearrange("p t m -> p (t m)")))
                hold(v)
                lk(v.tensor_copy(gval[k], sval[:, tiles].rearrange("p t m -> p (t m)")))
                assert lk.n == LKF
                v.sem_inc(gi_ok[k], 1)

            def weigh(k, n):
                v.wait_ge(s_gx[k], 16 * TB * KNN * (n + 1))
                i = v.tensor_tensor(gx[k], gx[k], bcast(gval[k], D), ALU.mult)
                i.then_inc(wt_ok[k], 1)
                v.wait_ge(wt_ok[k], n + 1)
                if not is_first(n):
                    v.wait_ge(u_ok[k], n)
                v.tensor_reduce(gs[k], gx[k].rearrange("p (j m) d -> p j d m", m=KNN), AX, ALU.add)\
                 .then_inc(gs_ok[k], 1)

            def finish(k, n):
                lk = Link(v, fin[k], LKD * n)
                ib = (HB + n) if k == HEAVY else n
                if k == LIGHT:
                    v.wait_ge(u_ok[k], n + 1)
                    if not is_first(n):
                        v.wait_ge(v_ok[k], n)
                    v.tensor_tensor(yf[k], PS[:, k], acc[:, bass.ds(n * BC, BC)], ALU.add).then_inc(yf_ok[k], 1)
                hold(v)
                lk(v.tensor_copy(gd2[k], d2s[:, bass.ds(ib * TB, TB)]))
                v.wait_ge(s_xb[k], 16 * (n + 1))
                lk(v.tensor_tensor(xb[k], xb[k], b2r[:, :].unsqueeze(1).to_broadcast([P, TB, D]), ALU.add))
                v.wait_ge(v_ok[k], n + 1)
                for j in range(TB):
                    i = v.scalar_tensor_tensor(xb[k][:, j], PS[:, 2 + k, j * P:(j + 1) * P], gd2[k][:, j:j + 1],
                                               xb[k][:, j], ALU.mult, ALU.add)
                lk(i)
                hold(v)
                for j in range(TB):
                    i = v.bn_stats(stats[k][:, j], xb[k][:, j])
                lk(i)
                hold(v)
                for j in range(TB):
                    i = v.bn_aggr(mv[k][:, j], stats[k][:, j])
                lk(i)
                v.tensor_scalar(mv[k][:, :, 1], mv[k][:, :, 1], LN_EPS, None, ALU.add).then_inc(var_ok[k], 1)
                v.wait_ge(std_ok[k], n + 1)
                lk(v.reciprocal(rstd[k], rstd[k]))
                if not is_first(n):
                    v.wait_ge(s_out[k], 16 * n)
                for j in range(TB):
                    i = v.tensor_scalar(res[k][:, j], xb[k][:, j], mv[k][:, j, 0:1], rstd[k][:, j:j + 1],
                                        ALU.subtract, ALU.mult)
                lk(i)
                assert lk.n == LKD
                v.sem_inc(out_ok[k], 1)

            fetch(LIGHT, 0)
            fetch(HEAVY, 0)

            def step_dve(s):
                for l in lights(s):
                    weigh(LIGHT, l)
                    if not (isinstance(l, int) and l == HB - 1):
                        fetch(LIGHT, l + 1)
                    finish(LIGHT, l)
                weigh(HEAVY, s)
                if not (isinstance(s, int) and s == B - HB - 1):
                    fetch(HEAVY, s + 1)
                finish(HEAVY, s)

            for s in range(TWO):
                step_dve(s)
            with v.Fori(TWO, B - HB - 1) as s:
                step_dve(s)
            step_dve(B - HB - 1)


def kernel(x, adj, L0_gnn_W1, L0_gnn_b1, L0_gnn_W2, L0_gnn_b2):
    import concourse.bacc as bacc
    from concourse.bass_utils import run_bass_kernel_spmd

    adj = np.asarray(adj)
    at = np.ascontiguousarray(adj.reshape(B, BC, T, P).transpose(0, 3, 2, 1))
    arrays = {
        "x": np.ascontiguousarray(x), "at": at,
        "W1": np.ascontiguousarray(L0_gnn_W1), "b1": np.ascontiguousarray(L0_gnn_b1),
        "W2": np.ascontiguousarray(L0_gnn_W2), "b2": np.ascontiguousarray(L0_gnn_b2),
        "consts": constants(),
    }
    nc = bacc.Bacc("TRN2", target_bir_lowering=False, num_devices=1)
    ins = {k: nc.dram_tensor(k, a.shape, F32, kind="ExternalInput").ap() for k, a in arrays.items()}
    out = nc.dram_tensor("out", (N, D), F32, kind="ExternalOutput").ap()
    xs_dram = nc.dram_tensor("xs_dram", (N, D), F32, kind="Internal").ap()
    build(nc, **ins, out=out, xs_dram=xs_dram)
    r = run_bass_kernel_spmd(nc, [arrays], core_ids=[0])
    return r.results[0]["out"]
```
